# Optimizing a Trainium2 kernel written in Bass

```python
import numpy as np
import jax
import jax.numpy as jnp

def _softmax(x, axis=-1):
    return jax.nn.softmax(x, axis=axis)

def _gelu(x):
    return jax.nn.gelu(x, approximate=True)

def _silu(x):
    return jax.nn.silu(x)

def _sigmoid(x):
    return jax.nn.sigmoid(x)

def _layernorm(x, axis=-1, eps=1e-05):
    m = jnp.mean(x, axis=axis, keepdims=True)
    v = jnp.var(x, axis=axis, keepdims=True)
    return (x - m) / jnp.sqrt(v + eps)

def _scatter_add(tgt, idx, src, axis=0):
    return tgt.at[idx].add(src)

def _segment_sum(src, seg, n):
    return jax.ops.segment_sum(src, seg, n)
kernel_name = 'mk_adj_preln_d2_adj_r2_0a3ae3'

def setup_inputs(seed: int=0):
    np.random.seed(seed)
    _w = jnp.asarray

    def _rec_inputs():
        import jax
        import jax.numpy as jnp
        _gk = jax.random.key(seed)
        x = -9.806e-05 + 1 * jax.random.normal(jax.random.fold_in(_gk, 1), (4096, 64), jnp.float32)
        _a = jax.random.bernoulli(jax.random.fold_in(_gk, 2), 0.000976562, (4096, 4096))
        _a = jnp.logical_or(_a, jnp.swapaxes(_a, -1, -2))
        _a = jnp.logical_or(_a, jnp.eye(4096, dtype=bool))
        adj = _a.astype(jnp.int32)
        return (x, adj)
    x, adj = _rec_inputs()

    def _L0_gnn_setup():
        import jax, jax.numpy as jnp
        import numpy as np
        ALPHA = 0.2
        NEG_BIG = -9000000000000000.0
        key = jax.random.key(seed)
        k1, k2, k3, k4, k5 = jax.random.split(key, 5)
        N, M, F_in, F_out = (4096, 4096, 64, 64)
        item_embs = jax.random.normal(k1, (N, F_in), dtype=jnp.float32)
        entity_embs = jax.random.normal(k2, (M, F_in), dtype=jnp.float32)
        adj = jax.random.randint(k3, (N, M), 0, 2, dtype=jnp.int32)
        W = jax.random.normal(k4, (F_in, F_out), dtype=jnp.float32)
        a = jax.random.normal(k5, (2 * F_out, 1), dtype=jnp.float32)
        return {'item_embs': item_embs, 'entity_embs': entity_embs, 'adj': adj, 'W': W, 'a': a}
    _L0_gnn_all = _L0_gnn_setup()
    _L0_gnn_in = {k: v for k, v in _L0_gnn_all.items() if k in ('entity_embs', 'W', 'a')}
    del _L0_gnn_all

    def _L1_gnn_setup():
        import jax, jax.numpy as jnp
        import numpy as np
        N = 8192
        D = 64
        key = jax.random.key(seed)
        kx, ka = jax.random.split(key)
        x = jax.random.normal(kx, (N, D), dtype=jnp.float32)
        adj = jax.random.randint(ka, (N, N), 0, 2, dtype=jnp.int32)
        return {'x': x, 'adj': adj}
    _L1_gnn_all = _L1_gnn_setup()
    _L1_gnn_in = {k: v for k, v in _L1_gnn_all.items() if k in ()}
    del _L1_gnn_all
    return {'x': x, 'adj': adj, 'L0_gnn_entity_embs': _L0_gnn_in['entity_embs'], 'L0_gnn_W': _L0_gnn_in['W'], 'L0_gnn_a': _L0_gnn_in['a']}

def reference(x, adj, L0_gnn_entity_embs, L0_gnn_W, L0_gnn_a):
    import jax
    import jax.numpy as jnp

    def _L0_gnn_ref(item_embs, entity_embs, adj, W, a):
        import jax, jax.numpy as jnp
        import numpy as np
        ALPHA = 0.2
        NEG_BIG = -9000000000000000.0
        F_out = W.shape[1]
        Wh = item_embs @ W
        We = entity_embs @ W
        a1 = a[:F_out, 0]
        a2 = a[F_out:, 0]
        scores = (Wh @ a1)[:, None] + (We @ a2)[None, :]
        e = jnp.where(scores > 0, scores, ALPHA * scores)
        e = jnp.where(adj > 0, e, NEG_BIG)
        attention = jax.nn.softmax(e, axis=1)
        entity_emb_weighted = attention @ entity_embs
        h_prime = entity_emb_weighted + item_embs
        return jax.nn.elu(h_prime)

    def _L1_gnn_ref(x, adj):
        import jax, jax.numpy as jnp
        import numpy as np
        N = 8192
        D = 64
        a = (adj == 1).astype(x.dtype)
        return jnp.matmul(a, x) + x
    h = jnp.maximum(_layernorm(x, axis=-1), 0.0)
    x = x + _L0_gnn_ref(h, L0_gnn_entity_embs, adj, L0_gnn_W, L0_gnn_a)
    h = jnp.maximum(_layernorm(x, axis=-1), 0.0)
    x = x + _L1_gnn_ref(h, adj)
    return x

_drawn_inputs = setup_inputs


def setup_inputs(seed=0):
    import zlib

    import numpy as np

    out = dict(_drawn_inputs(seed))
    spreads = {}
    factors = {}
    for name, (base, spread) in spreads.items():
        noise = np.random.default_rng([zlib.crc32(name.encode()), seed]).standard_normal(out[name].shape)
        drawn = base * np.exp(spread * noise) if base else spread * noise
        out[name] = jnp.asarray(drawn.astype(out[name].dtype))
    for name, factor in factors.items():
        out[name] = (out[name] * factor).astype(out[name].dtype)
    return out
```

```python
from contextlib import ExitStack

import concourse.bass as bass
from concourse import mybir

P = 128
F32 = mybir.dt.float32
BF16 = mybir.dt.bfloat16
FP8 = mybir.dt.float8e4
I32 = mybir.dt.int32
U8 = mybir.dt.uint8
ALU = mybir.AluOpType
ACT = mybir.ActivationFunctionType
X = mybir.AxisListType.X

BIG = 2.0 ** 53
ALPHA = 0.2
EPS = 1e-5
BLOCK = 512
SUB = BLOCK // P
CHUNK = 4
LANDS = 4
ZS = 4
PS = 4


def graph_layers(nc, adj_t, x, ent, ent_t, w_t, a_cols, eye, out, edges_dram, N, M, D):
    NB = N // BLOCK
    NT = M // P
    IT = N // P
    G = NT // CHUNK
    ACT_EDGES = {2, 5}
    dve_chunks = [g for g in range(G) if g not in ACT_EDGES]
    act_chunks = [g for g in range(G) if g in ACT_EDGES]

    ctx = ExitStack()
    with ctx:
        def sb(name, shape, dt):
            return ctx.enter_context(nc.sbuf_tensor(name, shape, dt))

        def ps(name, shape, dt=F32):
            return ctx.enter_context(nc.psum_tensor(name, shape, dt))

        def sem(name):
            return ctx.enter_context(nc.semaphore(name))

        land = sb("land", [P, LANDS, CHUNK * BLOCK], I32)
        pen = sb("pen", [P, 2, NT, BLOCK], BF16)
        stage = sb("stage", [P, LANDS, CHUNK * BLOCK], FP8)
        prob = sb("prob", [P, PS, BLOCK], F32)
        low = sb("low", [P, BLOCK], F32)
        s8 = sb("s8", [P, N], F32)
        xs = sb("xs", [P, IT, D], F32)
        h0 = sb("h0", [P, IT, D], F32)
        enta = sb("enta", [P, NT, D + 1], F32)
        h3 = sb("h3", [P, IT, 3 * D], BF16)
        vrow = sb("vrow", [3, 2, BLOCK], BF16)
        num_t = sb("num_t", [D + 1, BLOCK], F32)
        eyef = sb("eyef", [P, P], F32)
        eyeb = sb("eyeb", [P, P], BF16)
        neg_eye = sb("neg_eye", [P, P], BF16)
        onesf = sb("onesf", [P, P], F32)
        onesb = sb("onesb", [3, P], BF16)
        wt_sb = sb("wt_sb", [D, D], F32)
        a_sb = sb("a_sb", [D, 2], F32)
        w12 = sb("w12", [D, 2], F32)
        w1rep = sb("w1rep", [D, P], F32)
        tcol = sb("tcol", [P, NT], F32)
        t8neg = sb("t8neg", [P, NT], F32)
        scol = sb("scol", [P, IT], F32)
        stat = sb("stat", [P, 4, IT], F32)
        mhalf = sb("mhalf", [P, IT], F32)
        esum = sb("esum", [P, D + 1], F32)
        umin = sb("umin", [P, SUB], F32)
        lone = sb("lone", [P, 2, SUB], F32)
        vq = sb("vq", [P, 6, SUB], F32)
        v3 = sb("v3", [P, SUB, 3], BF16)
        nd = sb("nd", [P, SUB, D + 1], F32)
        rden = sb("rden", [P, SUB], F32)
        ea = sb("ea", [P, SUB, D], F32)
        eb = sb("eb", [P, SUB, D], F32)
        ec = sb("ec", [P, SUB, D], F32)
        est = sb("est", [P, 5, SUB], F32)
        early = pen[:, 1].rearrange("p t i -> p (t i)").bitcast(F32)
        ent_ts = early[0:D, 0:M]
        h0_t = early[0:D, M:M + N]
        sq = s8[:, 0:IT * D].rearrange("p (t d) -> p t d", d=D)
        edges = land[:, :, :].rearrange("p l n -> p (l n)").bitcast(FP8).rearrange(
            "p (k t i) -> p k t i", k=2, t=NT)
        ys = prob[:, :, :].rearrange("p k i -> p (k i)").rearrange("p (k c d) -> p k c d", k=PS * 2, d=D)

        bigh = sb("bigh", [P, 3], F32)
        sqr = sb("sqr", [P, CHUNK * BLOCK], BF16)

        z = ps("z", [P, ZS, BLOCK])
        acc = ps("acc", [P, BLOCK])
        low_t = ps("low_t", [P, SUB, P])
        vps = ps("vps", [P, BLOCK])
        ndps = ps("ndps", [P, BLOCK])

        loaded = sem("loaded")
        bigh_ready = sem("bigh_ready")
        landed = [sem(f"landed{k}") for k in range(LANDS)]
        stored = [sem(f"stored{k}") for k in range(LANDS)]
        edges_in = [sem(f"edges_in{k}") for k in range(2)]
        out_done = sem("out_done")
        consts = sem("consts")
        dve_chain = sem("dve_chain")
        act_chain = sem("act_chain")
        pool_chain = sem("pool_chain")
        w12_ps = sem("w12_ps")
        w12_sb = sem("w12_sb")
        t_ps = sem("t_ps")
        t_sb = sem("t_sb")
        esum_ps = sem("esum_ps")
        esum_sb = sem("esum_sb")
        var0 = sem("var0")
        rstd0 = sem("rstd0")
        h0_ready = sem("h0_ready")
        h0t_ps = sem("h0t_ps")
        h0t_sb = sem("h0t_sb")
        s_ps = sem("s_ps")
        s_sb = sem("s_sb")
        sc_ps = sem("sc_ps")
        sc_sb = sem("sc_sb")
        pen_made = sem("pen_made")
        edge_dve = sem("edge_dve")
        edge_act = sem("edge_act")
        low_done = sem("low_done")
        lowt_ps = sem("lowt_ps")
        umin_ready = sem("umin_ready")
        v3_ready = sem("v3_ready")
        v_ps = sem("v_ps")
        vrow_ready = sem("vrow_ready")
        z_ready = sem("z_ready")
        w_ready = sem("w_ready")
        exp_done = sem("exp_done")
        pv_done = sem("pv_done")
        num_sb = sem("num_sb")
        nd_ps = sem("nd_ps")
        nd_ready = sem("nd_ready")
        neg_ready = sem("neg_ready")
        expm_ready = sem("expm_ready")
        h_ready = sem("h_ready")
        sum_ps = sem("sum_ps")
        y_ready = sem("y_ready")

        def edge_count(n):
            q, r = n // G, n % G
            return (q * len(dve_chunks) + sum(g < r for g in dve_chunks),
                    q * len(act_chunks) + sum(g < r for g in act_chunks))

        def wait_edges(eng, n):
            d, a = edge_count(n)
            if d:
                eng.wait_ge(edge_dve, d)
            if a:
                eng.wait_ge(edge_act, a)

        def low_step(jt):
            return 2 + jt * 25 // NT

        def chunk_step(g):
            return max(0, low_step(g * CHUNK) - 1)

        LOW_END = low_step(NT - 1)

        block = ctx.enter_context(nc.Block())

        @block.sync
        def _(sp):
            for dst, src in ((wt_sb[:], w_t), (a_sb[:], a_cols), (eyef[:], eye), (ent_ts, ent_t),
                             (xs[:], x), (enta[:, :, 0:D], ent)):
                sp.dma_start(dst, src).then_inc(loaded, 16)

            def store_edges(n):
                k = n % LANDS
                wait_edges(sp, n + 1)
                sp.dma_start(edges_dram[n // G, :, (n % G) * CHUNK * BLOCK:(n % G + 1) * CHUNK * BLOCK],
                             stage[:, k].bitcast(U8)).then_inc(stored[k], 16)

            for n in range(NB * G):
                k = n % LANDS
                if n >= LANDS:
                    sp.wait_ge(pen_made, n - LANDS + 1)
                    wait_edges(sp, n - LANDS + 1)
                sp.dma_start(land[:, k], adj_t[n // G, n % G]).then_inc(landed[k], 16)
                if n >= LANDS:
                    store_edges(n - LANDS)
            for n in range(NB * G - LANDS, NB * G):
                store_edges(n)

            sp.wait_ge(pen_made, NB * G)
            for k in range(LANDS):
                sp.wait_ge(stored[k], 16 * NB * G // LANDS)
            for b in range(NB):
                if b >= 2:
                    sp.wait_ge(sum_ps, b - 1)
                sp.dma_start(edges[:, b % 2].bitcast(U8), edges_dram[b].rearrange("p (t i) -> p t i", t=NT)
                             ).then_inc(edges_in[b % 2], 16)

        @block.gpsimd
        def _(pool):
            g = nc.gpsimd
            steps = [0]

            def link(ins):
                steps[0] += 1
                ins.then_inc(pool_chain, 1)
                pool.wait_ge(pool_chain, steps[0])

            def chained(ins):
                steps[0] += 1
                return ins.then_inc(pool_chain, 1)

            g.memset(onesf[:], 1.0).then_inc(consts, 1)
            g.memset(onesb[:], 1.0).then_inc(consts, 1)
            link(g.memset(mhalf[:], -0.5))
            pool.wait_ge(loaded, 96)
            g.memset(enta[:, :, D:D + 1], 1.0).then_inc(consts, 1)
            pool.wait_ge(var0, 1)
            g.tensor_tensor(stat[:, 3], stat[:, 2], mhalf[:], ALU.pow).then_inc(rstd0, 1)

            def make_v(b):
                pool.wait_ge(umin_ready, b + 1)
                if b == 0:
                    pool.wait_ge(sc_sb, 1)
                if b >= 1:
                    pool.wait_ge(v_ps, b)
                s = scol[:, b * SUB:(b + 1) * SUB]
                link(g.tensor_tensor(vq[:, 0], s, umin[:], ALU.subtract))
                link(g.tensor_scalar(vq[:, 1], vq[:, 0], 1 - ALPHA, 0.0, ALU.mult, ALU.max))
                link(g.tensor_scalar(vq[:, 2], umin[:], ALPHA, None, ALU.mult))
                link(g.tensor_tensor(vq[:, 3], vq[:, 2], vq[:, 1], ALU.subtract))
                link(g.tensor_copy(v3[:, :, 0], vq[:, 3]))
                link(g.tensor_tensor(vq[:, 4], vq[:, 3], v3[:, :, 0], ALU.subtract))
                link(g.tensor_copy(v3[:, :, 1], vq[:, 4]))
                link(g.tensor_tensor(vq[:, 5], vq[:, 4], v3[:, :, 1], ALU.subtract))
                g.tensor_copy(v3[:, :, 2], vq[:, 5]).then_inc(v3_ready, 1)

            def row_sums(src, dst):
                w = D // 2
                link(g.tensor_tensor(eb[:, :, 0:w], src[:, :, 0:w], src[:, :, w:2 * w], ALU.add))
                while w > 2:
                    w //= 2
                    link(g.tensor_tensor(eb[:, :, 0:w], eb[:, :, 0:w], eb[:, :, w:2 * w], ALU.add))
                link(g.tensor_tensor(dst, eb[:, :, 0], eb[:, :, 1], ALU.add))

            def finish(b):
                t4 = slice(b * SUB, (b + 1) * SUB)

                def wide(col):
                    return col.unsqueeze(2).to_broadcast([P, SUB, D])

                pool.wait_ge(nd_ready, b + 1)
                link(g.tensor_tensor(ea[:], nd[:, :, 0:D], wide(rden[:]), ALU.mult))
                link(g.tensor_tensor(ea[:], ea[:], h0[:, t4], ALU.add))
                chained(g.tensor_scalar(eb[:], ea[:], 0.0, None, ALU.min))
                pool.wait_ge(pool_chain, steps[0])
                g.tensor_scalar(ec[:], ea[:], 0.0, None, ALU.max).then_inc(neg_ready, 1)
                pool.wait_ge(neg_ready, b + 1)
                link(g.tensor_tensor(ec[:], ec[:], xs[:, t4], ALU.add))
                pool.wait_ge(expm_ready, b + 1)
                link(g.tensor_scalar(ea[:], ea[:], 1.0, -1.0, ALU.mult, ALU.add))
                link(g.tensor_tensor(ec[:], ec[:], ea[:], ALU.add))
                row_sums(ec, est[:, 0])
                link(g.tensor_scalar(est[:, 1], est[:, 0], 1.0 / D, None, ALU.mult))
                link(g.tensor_tensor(ea[:], ec[:], wide(est[:, 1]), ALU.subtract))
                link(g.tensor_tensor(eb[:], ea[:], ea[:], ALU.mult))
                row_sums(eb, est[:, 2])
                link(g.tensor_scalar(est[:, 3], est[:, 2], 1.0 / D, EPS, ALU.mult, ALU.add))
                link(g.tensor_tensor(est[:, 4], est[:, 3], mhalf[:, 0:SUB], ALU.pow))
                link(g.tensor_tensor(ea[:], ea[:], wide(est[:, 4]), ALU.mult))
                link(g.tensor_scalar(ea[:], ea[:], 0.0, None, ALU.max))
                link(g.tensor_tensor(xs[:, t4], ec[:], ea[:], ALU.add))
                link(g.tensor_copy(h3[:, t4, 0:D], ea[:]))
                link(g.tensor_tensor(ea[:], ea[:], h3[:, t4, 0:D], ALU.subtract))
                link(g.tensor_copy(h3[:, t4, D:2 * D], ea[:]))
                link(g.tensor_tensor(ea[:], ea[:], h3[:, t4, D:2 * D], ALU.subtract))
                g.tensor_copy(h3[:, t4, 2 * D:3 * D], ea[:]).then_inc(h_ready, 1)
                pool.wait_ge(h_ready, b + 1)

            make_v(0)
            for b in range(NB):
                if b >= 1:
                    finish(b - 1)
                if b + 1 < NB:
                    make_v(b + 1)
            finish(NB - 1)

        @block.scalar
        def _(act):
            sc = nc.scalar
            act.wait_ge(loaded, 96)
            sc.copy(eyeb[:], eyef[:]).then_inc(consts, 1)
            sc.mul(neg_eye[:], eyef[:], -1.0).then_inc(consts, 1)
            act.wait_ge(w12_ps, 1)
            sc.copy(w12[:], acc[0:D, 0:2]).then_inc(act_chain, 1)
            act.wait_ge(act_chain, 1)
            act.wait_ge(consts, 5)
            sc.activation(w1rep[:], onesf[0:D, :], ACT.Copy, scale=w12[:, 0:1]).then_inc(w12_sb, 1)
            act.wait_ge(t_ps, 1)
            sc.copy(tcol[:], vps[:, 0:NT]).then_inc(t_sb, 1)
            sc.mul(t8neg[:], vps[:, 0:NT], ALPHA - 1.0).then_inc(t_sb, 1)
            act.wait_ge(esum_ps, 1)
            sc.copy(esum[:], ndps[:, 0:D + 1]).then_inc(esum_sb, 1)

            def penalties(b, gg):
                n = b * G + gg
                act.wait_ge(landed[n % LANDS], 16 * (n // LANDS + 1))
                if b >= 2:
                    act.wait_ge(z_ready, (b - 2) * NT + (gg + 1) * CHUNK)
                if b == 1 and gg == 0:
                    act.wait_ge(s_ps, NB)
                    act.wait_ge(sc_ps, 1)
                    act.wait_ge(t_ps, 1)
                sc.activation(pen[:, b % 2, gg * CHUNK:(gg + 1) * CHUNK].rearrange("p t i -> p (t i)"),
                              land[:, n % LANDS], ACT.Relu, scale=-BIG, bias=bigh[:, 0:1]).then_inc(pen_made, 1)
                if gg in ACT_EDGES:
                    if n >= LANDS:
                        act.wait_ge(stored[n % LANDS], 16 * (n // LANDS))
                    sc.activation(sqr[:], land[:, n % LANDS], ACT.Square, bias=bigh[:, 1:2]).then_inc(act_chain, 1)
                    chain[0] += 1
                    act.wait_ge(act_chain, chain[0])
                    sc.activation(stage[:, n % LANDS], sqr[:], ACT.Relu, scale=-1.0,
                                  bias=bigh[:, 2:3], saturate=False).then_inc(edge_act, 1)
                    act.wait_ge(edge_act, edge_count(n + 1)[1])

            chain = [1]
            act.wait_ge(bigh_ready, 1)
            penalties(0, 0)
            penalties(0, 1)
            for b in range(NB):
                act.wait_ge(h0t_ps, b + 1)
                sc.copy(h0_t[:, b * BLOCK:(b + 1) * BLOCK], z[0:D, b % 2]).then_inc(h0t_sb, 1)
                if b >= 1:
                    act.wait_ge(s_ps, b)
                    sc.mul(s8[:, (b - 1) * BLOCK:b * BLOCK], z[:, 2 + (b - 1) % 2], 1 - ALPHA).then_inc(s_sb, 1)
                if 2 + b < G:
                    penalties(0, 2 + b)
            act.wait_ge(s_ps, NB)
            sc.mul(s8[:, (NB - 1) * BLOCK:NB * BLOCK], z[:, 2 + (NB - 1) % 2], 1 - ALPHA).then_inc(s_sb, 1)
            act.wait_ge(sc_ps, 1)
            sc.copy(scol[:], vps[:, 0:IT]).then_inc(sc_sb, 1)

            def v_rows(b):
                act.wait_ge(v_ps, b + 1)
                if b >= 2:
                    act.wait_ge(z_ready, (b - 1) * NT)
                sc.copy(vrow[:, b % 2], vps[0:3, :]).then_inc(vrow_ready, 1)

            v_rows(0)
            for b in range(NB):
                for jt in range(NT):
                    if b + 1 < NB:
                        for gg in range(G):
                            if chunk_step(gg) == jt:
                                penalties(b + 1, gg)
                    n = b * NT + jt
                    act.wait_ge(w_ready, n + 1)
                    if n >= PS:
                        act.wait_ge(pv_done, n - PS + 1)
                    sc.activation(prob[:, jt % PS], z[:, jt % ZS], ACT.Exp, bias=tcol[:, jt:jt + 1]
                                  ).then_inc(exp_done, 1)
                    if b >= 1 and jt == 0:
                        act.wait_ge(pv_done, b * NT)
                        if b >= 2:
                            act.wait_ge(nd_ps, b - 1)
                        sc.copy(num_t[:], acc[0:D + 1, :]).then_inc(num_sb, 1)
                    if b >= 1 and jt == 12:
                        act.wait_ge(neg_ready, b)
                        sc.activation(ea[:], eb[:], ACT.Exp).then_inc(expm_ready, 1)
                    if b + 1 < NB and jt == NT - 2:
                        v_rows(b + 1)
            act.wait_ge(pv_done, NB * NT)
            act.wait_ge(nd_ps, NB - 1)
            sc.copy(num_t[:], acc[0:D + 1, :]).then_inc(num_sb, 1)
            act.wait_ge(neg_ready, NB)
            sc.activation(ea[:], eb[:], ACT.Exp).then_inc(expm_ready, 1)
            for b in range(NB):
                act.wait_ge(y_ready, b + 1)
                act.dma_start(out[:, b], ys[:, b]).then_inc(out_done, 16)
            act.wait_ge(out_done, 16 * NB)

        @block.vector
        def _(dve):
            v = nc.vector
            steps = [0]

            def link(ins):
                steps[0] += 1
                ins.then_inc(dve_chain, 1)
                dve.wait_ge(dve_chain, steps[0])

            link(v.memset(bigh[:, 0:1], BIG / 2))
            link(v.memset(bigh[:, 1:2], -1.0))
            v.memset(bigh[:, 2:3], 1.0).then_inc(bigh_ready, 1)

            def wide(col):
                return col.unsqueeze(2).to_broadcast([P, IT, D])

            dve.wait_ge(loaded, 96)
            link(v.tensor_reduce(stat[:, 0], xs[:], X, ALU.add))
            link(v.tensor_scalar(stat[:, 1], stat[:, 0], 1.0 / D, None, ALU.mult))
            link(v.tensor_tensor(h0[:], xs[:], wide(stat[:, 1]), ALU.subtract))
            link(v.tensor_tensor(sq, h0[:], h0[:], ALU.mult))
            link(v.tensor_reduce(stat[:, 0], sq, X, ALU.add))
            v.tensor_scalar(stat[:, 2], stat[:, 0], 1.0 / D, EPS, ALU.mult, ALU.add).then_inc(var0, 1)
            dve.wait_ge(rstd0, 1)
            link(v.tensor_tensor(h0[:], h0[:], wide(stat[:, 3]), ALU.mult))
            v.tensor_scalar(h0[:], h0[:], 0.0, None, ALU.max).then_inc(h0_ready, 1)
            dve.wait_ge(t_sb, 2)

            def edge_chunk(b, gg):
                n = b * G + gg
                if gg in ACT_EDGES:
                    return
                dve.wait_ge(landed[n % LANDS], 16 * (n // LANDS + 1))
                if n >= LANDS:
                    dve.wait_ge(stored[n % LANDS], 16 * (n // LANDS))
                v.tensor_scalar(stage[:, n % LANDS], land[:, n % LANDS], 1.0, None, ALU.is_equal,
                                saturate=False).then_inc(edge_dve, 1)

            def low_tile(b, jt):
                n = b * NT + jt
                dve.wait_ge(pen_made, b * G + jt // CHUNK + 1)
                tc = tcol[:, jt:jt + 1]
                if jt == 0:
                    if b >= 1:
                        dve.wait_ge(lowt_ps, b)
                    v.tensor_scalar(low[:], pen[:, b % 2, jt], tc, None, ALU.subtract).then_inc(low_done, 1)
                else:
                    dve.wait_ge(low_done, n)
                    v.scalar_tensor_tensor(out=low[:], in0=pen[:, b % 2, jt], scalar=tc, in1=low[:],
                                           op0=ALU.subtract, op1=ALU.min).then_inc(low_done, 1)

            def low_reduce(b):
                dve.wait_ge(lowt_ps, b + 1)
                if b >= 1:
                    dve.wait_ge(v3_ready, b)
                v.tensor_reduce(umin[:], low_t[:], X, ALU.min).then_inc(umin_ready, 1)
                dve.wait_ge(umin_ready, b + 1)
                link(v.tensor_scalar(lone[:, b % 2], umin[:], BIG / 4, None, ALU.is_gt))

            def numden(b):
                dve.wait_ge(nd_ps, b + 1)
                if b == 0:
                    dve.wait_ge(esum_sb, 1)
                if b >= 1:
                    dve.wait_ge(neg_ready, b)
                for c in range(SUB):
                    link(v.scalar_tensor_tensor(out=nd[:, c], in0=esum[:], scalar=lone[:, b % 2, c:c + 1],
                                                in1=ndps[:, c * (D + 1):(c + 1) * (D + 1)],
                                                op0=ALU.mult, op1=ALU.add))
                v.reciprocal(rden[:], nd[:, :, D]).then_inc(nd_ready, 1)

            for jt in range(NT):
                if jt % CHUNK == 0:
                    edge_chunk(0, jt // CHUNK)
                low_tile(0, jt)
            low_reduce(0)
            dve.wait_ge(s_sb, NB)
            for b in range(NB):
                for jt in range(NT):
                    n = b * NT + jt
                    dve.wait_ge(z_ready, n + 1)
                    v.scalar_tensor_tensor(out=z[:, jt % ZS], in0=s8[:, b * BLOCK:(b + 1) * BLOCK],
                                           scalar=t8neg[:, jt:jt + 1], in1=z[:, jt % ZS],
                                           op0=ALU.max, op1=ALU.add).then_inc(w_ready, 1)
                    if b >= 1 and jt == 4:
                        numden(b - 1)
                    if b + 1 < NB:
                        for gg in range(G):
                            if chunk_step(gg) + 1 == jt:
                                edge_chunk(b + 1, gg)
                        for q in range(NT):
                            if low_step(q) == jt:
                                low_tile(b + 1, q)
                        if jt == LOW_END + 1:
                            low_reduce(b + 1)
            numden(NB - 1)
            for b in range(NB):
                dve.wait_ge(sum_ps, b + 1)
                y = ys[:, b]
                zz = lambda k: z[:, :, k * D:(k + 1) * D]
                link(v.tensor_tensor(y, xs[:, b * SUB:(b + 1) * SUB], zz(2), ALU.add))
                link(v.tensor_tensor(y, y, zz(1), ALU.add))
                v.tensor_tensor(y, y, zz(0), ALU.add).then_inc(y_ready, 1)

        @block.tensor
        def _(pe):
            t = nc.tensor
            pe.wait_ge(loaded, 96)
            t.matmul(acc[0:D, 0:2], wt_sb[:], a_sb[:], start=True, stop=True).then_inc(w12_ps, 1)
            pe.wait_ge(w12_sb, 1)
            for jt in range(NT):
                mm = t.matmul(vps[:, jt:jt + 1], ent_ts[:, jt * P:(jt + 1) * P], w12[:, 1:2], start=True, stop=True)
            mm.then_inc(t_ps, 1)
            pe.wait_ge(consts, 5)
            for jt in range(NT):
                mm = t.matmul(ndps[:, 0:D + 1], onesf[:], enta[:, jt], start=(jt == 0), stop=(jt == NT - 1))
            mm.then_inc(esum_ps, 1)
            pe.wait_ge(h0_ready, 1)
            for b in range(NB):
                if b >= 2:
                    pe.wait_ge(h0t_sb, b - 1)
                for c in range(SUB):
                    mm = t.transpose(z[0:D, b % 2, c * P:(c + 1) * P], h0[:, b * SUB + c], eyef[:])
                mm.then_inc(h0t_ps, 1)
                if b >= 1:
                    pe.wait_ge(h0t_sb, b)
                    if b >= 3:
                        pe.wait_ge(s_sb, b - 2)
                    t.matmul(z[:, 2 + (b - 1) % 2], w1rep[:], h0_t[:, (b - 1) * BLOCK:b * BLOCK],
                             start=True, stop=True).then_inc(s_ps, 1)
            pe.wait_ge(h0t_sb, NB)
            pe.wait_ge(s_sb, NB - 2)
            t.matmul(z[:, 2 + (NB - 1) % 2], w1rep[:], h0_t[:, (NB - 1) * BLOCK:NB * BLOCK],
                     start=True, stop=True).then_inc(s_ps, 1)
            pe.wait_ge(t_sb, 2)
            for c in range(IT):
                mm = t.matmul(vps[:, c:c + 1], h0_t[:, c * P:(c + 1) * P], w12[:, 0:1], start=True, stop=True)
            mm.then_inc(sc_ps, 1)

            def low_transpose(b):
                pe.wait_ge(low_done, (b + 1) * NT)
                if b >= 1:
                    pe.wait_ge(umin_ready, b)
                for c in range(SUB):
                    mm = t.transpose(low_t[:, c], low[:, c * P:(c + 1) * P], eyef[:])
                mm.then_inc(lowt_ps, 1)

            def v_rows(b):
                pe.wait_ge(v3_ready, b + 1)
                if b == 0:
                    pe.wait_ge(sc_sb, 1)
                else:
                    pe.wait_ge(vrow_ready, b)
                for c in range(SUB):
                    mm = t.matmul(vps[0:3, c * P:(c + 1) * P], v3[:, c, :], eyeb[:], start=True, stop=True)
                mm.then_inc(v_ps, 1)

            def scores(n):
                b, jt = n // NT, n % NT
                if jt == 0:
                    pe.wait_ge(vrow_ready, b + 1)
                if n == 0:
                    pe.wait_ge(s_sb, NB)
                if n >= ZS:
                    pe.wait_ge(exp_done, n - ZS + 1)
                t.matmul(z[:, jt % ZS], neg_eye[:], pen[:, b % 2, jt], start=True, stop=False)
                t.matmul(z[:, jt % ZS], onesb[:], vrow[:, b % 2], start=False, stop=True).then_inc(z_ready, 1)

            def numden_t(b):
                pe.wait_ge(num_sb, b + 1)
                if b >= 1:
                    pe.wait_ge(nd_ready, b)
                else:
                    pe.wait_ge(esum_sb, 1)
                for c in range(SUB):
                    mm = t.transpose(ndps[:, c * (D + 1):(c + 1) * (D + 1)], num_t[:, c * P:(c + 1) * P],
                                     eyef[0:D + 1, 0:D + 1])
                mm.then_inc(nd_ps, 1)

            low_transpose(0)
            v_rows(0)
            AHEAD = ZS - 1
            for n in range(AHEAD):
                scores(n)
            for b in range(NB):
                for jt in range(NT):
                    n = b * NT + jt
                    if b + 1 < NB and jt == LOW_END + 1:
                        low_transpose(b + 1)
                    if b + 1 < NB and jt == NT - AHEAD:
                        v_rows(b + 1)
                    if n + AHEAD < NB * NT:
                        scores(n + AHEAD)
                    pe.wait_ge(exp_done, n + 1)
                    if jt == 0 and b >= 1:
                        pe.wait_ge(num_sb, b)
                    t.matmul(acc[0:D + 1, :], enta[:, jt], prob[:, jt % PS], start=(jt == 0), stop=(jt == NT - 1)
                             ).then_inc(pv_done, 1)
                    if b >= 1 and jt == 2:
                        numden_t(b - 1)
            numden_t(NB - 1)
            pe.wait_ge(h_ready, NB)
            pe.wait_ge(exp_done, NB * NT)
            for b in range(NB):
                pe.wait_ge(edges_in[b % 2], 16 * (b // 2 + 1))
                if b >= 1:
                    pe.wait_ge(y_ready, b)
                for c in range(SUB):
                    for jt in range(NT):
                        mm = t.matmul(z[:, c, 0:3 * D], edges[:, b % 2, jt, c * P:(c + 1) * P], h3[:, jt],
                                      start=(jt == 0), stop=(jt == NT - 1))
                mm.then_inc(sum_ps, 1)


def kernel(x, adj, L0_gnn_entity_embs, L0_gnn_W, L0_gnn_a):
    import numpy as np
    import concourse.bacc as bacc
    from concourse.bass_utils import run_bass_kernel_spmd

    N, D = x.shape
    M = adj.shape[1]
    NB, NT, IT = N // BLOCK, M // P, N // P
    G = NT // CHUNK

    def rows(a):
        return np.ascontiguousarray(np.asarray(a).reshape(-1, P, D).transpose(1, 0, 2))

    a = np.asarray(adj).reshape(NB, BLOCK, G, CHUNK, P).transpose(0, 2, 4, 3, 1)
    arrays = {
        "adj_t": np.ascontiguousarray(a).reshape(NB, G, P, CHUNK * BLOCK),
        "x": rows(x),
        "ent": rows(L0_gnn_entity_embs),
        "ent_t": np.ascontiguousarray(np.asarray(L0_gnn_entity_embs).T),
        "w_t": np.ascontiguousarray(np.asarray(L0_gnn_W).T),
        "a_cols": np.ascontiguousarray(np.asarray(L0_gnn_a).reshape(2, D).T),
        "eye": np.eye(P, dtype=np.float32),
    }
    nc = bacc.Bacc("TRN2", target_bir_lowering=False, num_devices=1)
    ins = {k: nc.dram_tensor(k, v.shape, mybir.dt.from_np(v.dtype), kind="ExternalInput").ap()
           for k, v in arrays.items()}
    out = nc.dram_tensor("out", (P, NB, SUB, D), F32, kind="ExternalOutput").ap()
    edges_dram = nc.dram_tensor("edges_dram", (NB, P, NT * BLOCK), U8, kind="Internal").ap()
    graph_layers(nc, out=out, edges_dram=edges_dram, N=N, M=M, D=D, **ins)
    r = run_bass_kernel_spmd(nc, [arrays], core_ids=[0])
    got = r.results[0]["out"].reshape(P, IT, D)
    return np.ascontiguousarray(got.transpose(1, 0, 2)).reshape(N, D)
```
